# Optimizing a Trainium2 kernel written in Bass

```python
import numpy as np
import jax
import jax.numpy as jnp

def _softmax(x, axis=-1):
    return jax.nn.softmax(x, axis=axis)

def _gelu(x):
    return jax.nn.gelu(x, approximate=True)

def _silu(x):
    return jax.nn.silu(x)

def _sigmoid(x):
    return jax.nn.sigmoid(x)

def _layernorm(x, axis=-1, eps=1e-05):
    m = jnp.mean(x, axis=axis, keepdims=True)
    v = jnp.var(x, axis=axis, keepdims=True)
    return (x - m) / jnp.sqrt(v + eps)

def _scatter_add(tgt, idx, src, axis=0):
    return tgt.at[idx].add(src)

def _segment_sum(src, seg, n):
    return jax.ops.segment_sum(src, seg, n)
kernel_name = 'mk_dlrm_tower_d1_rec_r8_1dcc26'

def setup_inputs(seed: int=0):
    np.random.seed(seed)
    _w = jnp.asarray

    def _rec_inputs():
        import jax
        import jax.numpy as jnp
        _tk = jax.random.key(seed)
        dense_ctx = jax.random.normal(jax.random.fold_in(_tk, 190), (512, 16), jnp.float32)
        ids = jnp.stack([jax.random.randint(jax.random.fold_in(_tk, 200 + f), (512,), 0, v, jnp.int32) for f, v in enumerate([12500, 1250, 12500, 1000, 12500, 1250, 1250, 1250, 1250, 12500, 12500, 1250, 1000, 1000, 1250, 1250, 12500, 12500, 1250, 1000, 12500, 1250, 1250, 1250, 1000, 1250, 1250, 1250, 1000, 1000, 1000, 1250])], axis=1)
        tbl_0 = 0.05 * jax.random.normal(jax.random.fold_in(_tk, 500 + 0), (12500, 256), jnp.float32)
        tbl_1 = 0.05 * jax.random.normal(jax.random.fold_in(_tk, 500 + 1), (1250, 256), jnp.float32)
        tbl_2 = 0.05 * jax.random.normal(jax.random.fold_in(_tk, 500 + 2), (12500, 256), jnp.float32)
        tbl_3 = 0.05 * jax.random.normal(jax.random.fold_in(_tk, 500 + 3), (1000, 256), jnp.float32)
        tbl_4 = 0.05 * jax.random.normal(jax.random.fold_in(_tk, 500 + 4), (12500, 256), jnp.float32)
        tbl_5 = 0.05 * jax.random.normal(jax.random.fold_in(_tk, 500 + 5), (1250, 256), jnp.float32)
        tbl_6 = 0.05 * jax.random.normal(jax.random.fold_in(_tk, 500 + 6), (1250, 256), jnp.float32)
        tbl_7 = 0.05 * jax.random.normal(jax.random.fold_in(_tk, 500 + 7), (1250, 256), jnp.float32)
        tbl_8 = 0.05 * jax.random.normal(jax.random.fold_in(_tk, 500 + 8), (1250, 256), jnp.float32)
        tbl_9 = 0.05 * jax.random.normal(jax.random.fold_in(_tk, 500 + 9), (12500, 256), jnp.float32)
        tbl_10 = 0.05 * jax.random.normal(jax.random.fold_in(_tk, 500 + 10), (12500, 256), jnp.float32)
        tbl_11 = 0.05 * jax.random.normal(jax.random.fold_in(_tk, 500 + 11), (1250, 256), jnp.float32)
        tbl_12 = 0.05 * jax.random.normal(jax.random.fold_in(_tk, 500 + 12), (1000, 256), jnp.float32)
        tbl_13 = 0.05 * jax.random.normal(jax.random.fold_in(_tk, 500 + 13), (1000, 256), jnp.float32)
        tbl_14 = 0.05 * jax.random.normal(jax.random.fold_in(_tk, 500 + 14), (1250, 256), jnp.float32)
        tbl_15 = 0.05 * jax.random.normal(jax.random.fold_in(_tk, 500 + 15), (1250, 256), jnp.float32)
        tbl_16 = 0.05 * jax.random.normal(jax.random.fold_in(_tk, 500 + 16), (12500, 256), jnp.float32)
        tbl_17 = 0.05 * jax.random.normal(jax.random.fold_in(_tk, 500 + 17), (12500, 256), jnp.float32)
        tbl_18 = 0.05 * jax.random.normal(jax.random.fold_in(_tk, 500 + 18), (1250, 256), jnp.float32)
        tbl_19 = 0.05 * jax.random.normal(jax.random.fold_in(_tk, 500 + 19), (1000, 256), jnp.float32)
        tbl_20 = 0.05 * jax.random.normal(jax.random.fold_in(_tk, 500 + 20), (12500, 256), jnp.float32)
        tbl_21 = 0.05 * jax.random.normal(jax.random.fold_in(_tk, 500 + 21), (1250, 256), jnp.float32)
        tbl_22 = 0.05 * jax.random.normal(jax.random.fold_in(_tk, 500 + 22), (1250, 256), jnp.float32)
        tbl_23 = 0.05 * jax.random.normal(jax.random.fold_in(_tk, 500 + 23), (1250, 256), jnp.float32)
        tbl_24 = 0.05 * jax.random.normal(jax.random.fold_in(_tk, 500 + 24), (1000, 256), jnp.float32)
        tbl_25 = 0.05 * jax.random.normal(jax.random.fold_in(_tk, 500 + 25), (1250, 256), jnp.float32)
        tbl_26 = 0.05 * jax.random.normal(jax.random.fold_in(_tk, 500 + 26), (1250, 256), jnp.float32)
        tbl_27 = 0.05 * jax.random.normal(jax.random.fold_in(_tk, 500 + 27), (1250, 256), jnp.float32)
        tbl_28 = 0.05 * jax.random.normal(jax.random.fold_in(_tk, 500 + 28), (1000, 256), jnp.float32)
        tbl_29 = 0.05 * jax.random.normal(jax.random.fold_in(_tk, 500 + 29), (1000, 256), jnp.float32)
        tbl_30 = 0.05 * jax.random.normal(jax.random.fold_in(_tk, 500 + 30), (1000, 256), jnp.float32)
        tbl_31 = 0.05 * jax.random.normal(jax.random.fold_in(_tk, 500 + 31), (1250, 256), jnp.float32)
        _rk = jax.random.fold_in(_tk, 7)
        W_top1 = 0.0441942 * jax.random.normal(jax.random.fold_in(_tk, 801), (512, 512), jnp.float32)
        W_top2 = 0.0441942 * jax.random.normal(jax.random.fold_in(_tk, 802), (512, 256), jnp.float32)
        W_top3 = 0.0625 * jax.random.normal(jax.random.fold_in(_tk, 803), (256, 1), jnp.float32)
        b_top1 = jnp.zeros((512,), jnp.float32)
        b_top2 = jnp.zeros((256,), jnp.float32)
        return (dense_ctx, ids, tbl_0, tbl_1, tbl_2, tbl_3, tbl_4, tbl_5, tbl_6, tbl_7, tbl_8, tbl_9, tbl_10, tbl_11, tbl_12, tbl_13, tbl_14, tbl_15, tbl_16, tbl_17, tbl_18, tbl_19, tbl_20, tbl_21, tbl_22, tbl_23, tbl_24, tbl_25, tbl_26, tbl_27, tbl_28, tbl_29, tbl_30, tbl_31, W_top1, b_top1, W_top2, b_top2, W_top3)
    dense_ctx, ids, tbl_0, tbl_1, tbl_2, tbl_3, tbl_4, tbl_5, tbl_6, tbl_7, tbl_8, tbl_9, tbl_10, tbl_11, tbl_12, tbl_13, tbl_14, tbl_15, tbl_16, tbl_17, tbl_18, tbl_19, tbl_20, tbl_21, tbl_22, tbl_23, tbl_24, tbl_25, tbl_26, tbl_27, tbl_28, tbl_29, tbl_30, tbl_31, W_top1, b_top1, W_top2, b_top2, W_top3 = _rec_inputs()

    def _L0_rec_setup():
        import jax, jax.numpy as jnp
        import numpy as np
        B, N, D = (1024, 32, 256)
        key = jax.random.key(seed)
        x = jax.random.normal(key, (B, N, D), dtype=jnp.float32)
        return {'x': x}
    _L0_rec_all = _L0_rec_setup()
    _L0_rec_in = {k: v for k, v in _L0_rec_all.items() if k in ()}
    del _L0_rec_all
    return {'dense_ctx': dense_ctx, 'ids': ids, 'tbl_0': tbl_0, 'tbl_1': tbl_1, 'tbl_2': tbl_2, 'tbl_3': tbl_3, 'tbl_4': tbl_4, 'tbl_5': tbl_5, 'tbl_6': tbl_6, 'tbl_7': tbl_7, 'tbl_8': tbl_8, 'tbl_9': tbl_9, 'tbl_10': tbl_10, 'tbl_11': tbl_11, 'tbl_12': tbl_12, 'tbl_13': tbl_13, 'tbl_14': tbl_14, 'tbl_15': tbl_15, 'tbl_16': tbl_16, 'tbl_17': tbl_17, 'tbl_18': tbl_18, 'tbl_19': tbl_19, 'tbl_20': tbl_20, 'tbl_21': tbl_21, 'tbl_22': tbl_22, 'tbl_23': tbl_23, 'tbl_24': tbl_24, 'tbl_25': tbl_25, 'tbl_26': tbl_26, 'tbl_27': tbl_27, 'tbl_28': tbl_28, 'tbl_29': tbl_29, 'tbl_30': tbl_30, 'tbl_31': tbl_31, 'W_top1': W_top1, 'b_top1': b_top1, 'W_top2': W_top2, 'b_top2': b_top2, 'W_top3': W_top3}

def reference(dense_ctx, ids, tbl_0, tbl_1, tbl_2, tbl_3, tbl_4, tbl_5, tbl_6, tbl_7, tbl_8, tbl_9, tbl_10, tbl_11, tbl_12, tbl_13, tbl_14, tbl_15, tbl_16, tbl_17, tbl_18, tbl_19, tbl_20, tbl_21, tbl_22, tbl_23, tbl_24, tbl_25, tbl_26, tbl_27, tbl_28, tbl_29, tbl_30, tbl_31, W_top1, b_top1, W_top2, b_top2, W_top3):
    import jax
    import jax.numpy as jnp

    def _L0_rec_ref(x):
        import jax, jax.numpy as jnp
        import numpy as np
        B, N, D = (1024, 32, 256)
        'Second-order feature interaction (DLRM dot interaction).\n\n            Computes dot(x_i, x_j) for all field pairs i < j (self_interaction=False),\n            flattened in row-major upper-triangular order -> [B, N*(N-1)/2].\n            Matches tf.boolean_mask(dot_products, strictly_upper_mask) ordering.\n            '
        b, n, d = x.shape
        iu, ju = jnp.triu_indices(n, k=1)
        dots = jnp.einsum('bnd,bmd->bnm', x, x)
        return dots[:, iu, ju]
    e = jnp.stack([tbl_0[ids[:, 0]], tbl_1[ids[:, 1]], tbl_2[ids[:, 2]], tbl_3[ids[:, 3]], tbl_4[ids[:, 4]], tbl_5[ids[:, 5]], tbl_6[ids[:, 6]], tbl_7[ids[:, 7]], tbl_8[ids[:, 8]], tbl_9[ids[:, 9]], tbl_10[ids[:, 10]], tbl_11[ids[:, 11]], tbl_12[ids[:, 12]], tbl_13[ids[:, 13]], tbl_14[ids[:, 14]], tbl_15[ids[:, 15]], tbl_16[ids[:, 16]], tbl_17[ids[:, 17]], tbl_18[ids[:, 18]], tbl_19[ids[:, 19]], tbl_20[ids[:, 20]], tbl_21[ids[:, 21]], tbl_22[ids[:, 22]], tbl_23[ids[:, 23]], tbl_24[ids[:, 24]], tbl_25[ids[:, 25]], tbl_26[ids[:, 26]], tbl_27[ids[:, 27]], tbl_28[ids[:, 28]], tbl_29[ids[:, 29]], tbl_30[ids[:, 30]], tbl_31[ids[:, 31]]], axis=1)
    z = _L0_rec_ref(e)
    z = z.reshape(z.shape[0], -1)
    h = jnp.concatenate([z, dense_ctx], axis=1)
    h = jnp.maximum(h @ W_top1 + b_top1, 0.0)
    h = jnp.maximum(h @ W_top2 + b_top2, 0.0)
    y = h @ W_top3
    return y

_drawn_inputs = setup_inputs


def setup_inputs(seed=0):
    import zlib

    import numpy as np

    out = dict(_drawn_inputs(seed))
    spreads = {'b_top1': (0.0, 0.1), 'b_top2': (0.0, 0.1)}
    factors = {}
    for name, (base, spread) in spreads.items():
        noise = np.random.default_rng([zlib.crc32(name.encode()), seed]).standard_normal(out[name].shape)
        drawn = base * np.exp(spread * noise) if base else spread * noise
        out[name] = jnp.asarray(drawn.astype(out[name].dtype))
    for name, factor in factors.items():
        out[name] = (out[name] * factor).astype(out[name].dtype)
    return out
```

```python
from contextlib import ExitStack

import concourse.bass as bass
import numpy as np
from concourse import mybir

F32 = mybir.dt.float32
I32 = mybir.dt.int32
ALU = mybir.AluOpType
ACT = mybir.ActivationFunctionType

P = 128
B = 512
F = 32
D = 256
KD = D // P
CTX = 16
H1, H2 = 512, 256
KH1, KH2 = H1 // P, H2 // P
J = P // F
HALF = 64
NH = B // HALF
G = HALF // J
PAIRS = G // 2
UNIT = 4
SLOTS = G
XT_SLOTS = 4
Q = 4
MM = F // Q


def halves(engine, half):
    half(0, 0, True, False)
    with engine.Fori(0, (NH - 2) // 2) as turn:
        half(turn * 2 + 1, 1, False, False)
        half(turn * 2 + 2, 0, False, False)
    half(NH - 1, 1, False, True)


def dlrm_tower(nc, table, ids, base, eye, ctx_t, w1z, w1c, b1, w2, b2, w3, y):
    with ExitStack() as stack:
        def sbuf(name, shape, dt=F32):
            return stack.enter_context(nc.sbuf_tensor(name, shape, dt))

        def psum(name, shape):
            return stack.enter_context(nc.psum_tensor(name, shape, F32))

        def sem(name):
            return stack.enter_context(nc.semaphore(name))

        ids_sb = sbuf("ids_sb", [P, B // J], I32)
        base_sb = sbuf("base_sb", [P, B // J], I32)
        row_number = sbuf("row_number", [P, B // J], I32)
        rows = sbuf("rows", [P, SLOTS, D])
        identity = sbuf("identity", [P, P])
        xt = sbuf("xt", [P, XT_SLOTS, 2, KD, P])
        z = sbuf("z", [P, 2, MM, HALF])
        ctx_sb = sbuf("ctx_sb", [CTX, B])
        w1z_sb = sbuf("w1z_sb", [P, MM, H1])
        w1c_sb = sbuf("w1c_sb", [CTX, H1])
        w2_sb = sbuf("w2_sb", [P, KH1, H2])
        w3_sb = sbuf("w3_sb", [P, KH2])
        b1_sb = sbuf("b1_sb", [P, KH1])
        b2_sb = sbuf("b2_sb", [P, KH2])
        h1_sb = sbuf("h1_sb", [P, KH1, HALF])
        h2_sb = sbuf("h2_sb", [P, KH2, HALF])
        y_sb = sbuf("y_sb", [1, B])

        xt_ps = [psum(f"xt_ps{i}", [P, 2, KD, P]) for i in range(2)]
        gram_ps = [psum(f"gram_ps{i}", [P, 2 * UNIT, P]) for i in range(2)]
        h1_ps = psum("h1_ps", [P, 512])
        h2_ps = psum("h2_ps", [P, 512])

        ids_loaded = sem("ids_loaded")
        ctx_loaded = sem("ctx_loaded")
        w1_loaded = sem("w1_loaded")
        w23_loaded = sem("w23_loaded")
        identity_loaded = sem("identity_loaded")
        numbered = sem("numbered")
        rows_landed = [sem(f"rows_landed{i}") for i in range(SLOTS)]
        rows_transposed = sem("rows_transposed")
        xt_ready = [sem("xt_even_ready"), sem("xt_odd_ready")]
        gram_ready = sem("gram_ready")
        z_dve = sem("z_dve")
        z_act = sem("z_act")
        h1_done = sem("h1_done")
        h1_ready = sem("h1_ready")
        h2_done = sem("h2_done")
        h2_ready = sem("h2_ready")
        y_done = sem("y_done")
        y_ready = sem("y_ready")
        y_stored = sem("y_stored")

        block = stack.enter_context(nc.Block())

        @block.sync
        def _(sp):
            sp.dma_start(ids_sb[:], ids).then_inc(ids_loaded, 16)
            sp.dma_start(base_sb[:], base).then_inc(ids_loaded, 16)
            sp.dma_start(identity[:], eye).then_inc(identity_loaded, 16)
            sp.dma_start(ctx_sb[:], ctx_t).then_inc(ctx_loaded, 16)
            sp.dma_start(w1c_sb[:], w1c).then_inc(ctx_loaded, 16)
            sp.dma_start(w1z_sb[:], w1z).then_inc(w1_loaded, 16)
            sp.dma_start(b1_sb[:], b1).then_inc(w23_loaded, 16)
            sp.dma_start(b2_sb[:], b2).then_inc(w23_loaded, 16)
            sp.dma_start(w2_sb[:], w2.rearrange("(k p) n -> p k n", p=P)).then_inc(w23_loaded, 16)
            sp.dma_start(w3_sb[:], w3).then_inc(w23_loaded, 16)
            sp.wait_ge(y_ready, NH + 1)
            sp.dma_start(y.rearrange("b o -> o b"), y_sb[:]).then_inc(y_stored, 16)
            sp.wait_ge(y_stored, 16)

        @block.gpsimd
        def _(pool):
            pool.wait_ge(numbered, 1)
            for n in range(B // J):
                if n >= SLOTS:
                    pool.wait_ge(rows_transposed, n + 1 - SLOTS)
                nc.gpsimd.indirect_dma_start(
                    rows[:, n % SLOTS, :], None, table,
                    bass.IndirectOffsetOnAxis(ap=row_number[:, n:n + 1], axis=0),
                ).then_inc(rows_landed[n % SLOTS], 16)

        def copy_xt(engine, copy, h, i, first):
            if not first or i >= XT_SLOTS:
                engine.wait_ge(gram_ready, h * PAIRS + (i + 1 - XT_SLOTS))
            engine.wait_ge(rows_transposed, h * G + 2 * (i + 1))
            copy(xt[:, i % XT_SLOTS], xt_ps[i % 2][:]).then_inc(xt_ready[i % 2], 1)

        def regroup(engine, copy, quadrants, done, h, parity, u, first):
            engine.wait_ge(gram_ready, h * PAIRS + UNIT * (u + 1))
            if u == 0 and not first:
                engine.wait_ge(h1_done, h)
            zv = z[:, parity].rearrange("p m (g j) -> p m g j", j=J)
            for j in quadrants:
                block_j = gram_ps[u][F * j:F * j + F, :, F * j:F * j + F].rearrange("p g (m q) -> p m g q", q=Q)
                for q in range(Q):
                    last = copy(zv[F * q:F * q + F, :, 2 * UNIT * u:2 * UNIT * (u + 1), j], block_j[:, :, :, q])
            last.then_inc(done, 1)

        @block.vector
        def _(dve):
            copy = nc.vector.tensor_copy

            def relu2(h):
                dve.wait_ge(w23_loaded, 64)
                dve.wait_ge(h2_done, h + 2)
                dve.wait_ge(y_done, h + 1)
                for k in range(KH2):
                    last = nc.vector.tensor_scalar(h2_sb[:, k, :], h2_ps[:, k * HALF:(k + 1) * HALF],
                                                   b2_sb[:, k:k + 1], 0.0, ALU.add, ALU.max)
                last.then_inc(h2_ready, 1)

            def keep_y(h):
                dve.wait_ge(y_done, h + 2)
                copy(y_sb[0:1, bass.ds(h * HALF, HALF)], h2_ps[0:1, KH2 * HALF:(KH2 + 1) * HALF]).then_inc(y_ready, 1)

            def half(h, parity, first, last):
                copy_xt(dve, copy, h, 0, first)
                if not first:
                    regroup(dve, copy, (0, 1), z_dve, h - 1, 1 - parity, 1, False)
                copy_xt(dve, copy, h, 2, first)
                copy_xt(dve, copy, h, 4, first)
                regroup(dve, copy, (0, 1), z_dve, h, parity, 0, first)
                if not first:
                    relu2(h - 1)
                copy_xt(dve, copy, h, 6, first)
                if not first:
                    keep_y(h - 1)

            nc.vector.nop().then_inc(y_ready, 1)
            dve.wait_ge(ids_loaded, 32)
            nc.vector.tensor_tensor(row_number[:], ids_sb[:], base_sb[:], ALU.add).then_inc(numbered, 1)
            halves(nc.vector, half)
            regroup(dve, copy, (0, 1), z_dve, NH - 1, 1, 1, False)
            relu2(NH - 1)
            keep_y(NH - 1)

        @block.scalar
        def _(act):
            copy = nc.scalar.copy

            def relu1(h):
                act.wait_ge(w23_loaded, 64)
                act.wait_ge(h1_done, h + 2)
                act.wait_ge(h2_done, h + 1)
                for k in range(KH1):
                    last = nc.scalar.activation(h1_sb[:, k, :], h1_ps[:, k * HALF:(k + 1) * HALF], ACT.Relu,
                                                bias=b1_sb[:, k:k + 1])
                last.then_inc(h1_ready, 1)

            def half(h, parity, first, last):
                if not first:
                    regroup(act, copy, (2, 3), z_act, h - 1, 1 - parity, 1, False)
                copy_xt(act, copy, h, 1, first)
                copy_xt(act, copy, h, 3, first)
                if not first:
                    relu1(h - 1)
                regroup(act, copy, (2, 3), z_act, h, parity, 0, first)
                copy_xt(act, copy, h, 5, first)
                copy_xt(act, copy, h, 7, first)

            nc.scalar.nop().then_inc(h1_ready, 1)
            halves(nc.scalar, half)
            regroup(act, copy, (2, 3), z_act, NH - 1, 1, 1, False)
            relu1(NH - 1)

        @block.tensor
        def _(pe):
            def transposes(h, i):
                pe.wait_ge(xt_ready[i % 2], h * (PAIRS // 2) + i // 2)
                for r in range(2):
                    g = 2 * i + r
                    pe.wait_ge(rows_landed[g], (h + 1) * 16)
                    for k in range(KD):
                        last = nc.tensor.transpose(xt_ps[i % 2][:, r, k, :], rows[:, g, k * P:(k + 1) * P], identity[:])
                    last.then_inc(rows_transposed, 1)

            def gram(h, i, first):
                u = i // UNIT
                pe.wait_ge(xt_ready[i % 2], h * (PAIRS // 2) + i // 2 + 1)
                if i % UNIT == 0 and (u or not first):
                    pe.wait_ge(z_dve, h * 2 + (u - 1))
                    pe.wait_ge(z_act, h * 2 + (u - 1))
                for r in range(2):
                    for k in range(KD):
                        x = xt[:, i % XT_SLOTS, r, k, :]
                        last = nc.tensor.matmul(gram_ps[u][:, 2 * (i % UNIT) + r, :], x, x, start=(k == 0),
                                                stop=(k == KD - 1))
                last.then_inc(gram_ready, 1)

            def layer1(h, parity):
                pe.wait_ge(ctx_loaded, 32)
                pe.wait_ge(w1_loaded, 16)
                pe.wait_ge(z_dve, h * 2 + 2)
                pe.wait_ge(z_act, h * 2 + 2)
                pe.wait_ge(h1_ready, h + 1)
                for n in range(KH1):
                    out = h1_ps[:, n * HALF:(n + 1) * HALF]
                    nc.tensor.matmul(out, w1c_sb[:, n * P:(n + 1) * P], ctx_sb[:, bass.ds(h * HALF, HALF)],
                                     start=True, stop=False)
                    for m in range(MM):
                        last = nc.tensor.matmul(out, w1z_sb[:, m, n * P:(n + 1) * P], z[:, parity, m, :], start=False,
                                                stop=(m == MM - 1))
                last.then_inc(h1_done, 1)

            def layer2(h):
                pe.wait_ge(w23_loaded, 64)
                pe.wait_ge(h1_ready, h + 2)
                pe.wait_ge(y_ready, h + 1)
                for n in range(KH2):
                    for k in range(KH1):
                        last = nc.tensor.matmul(h2_ps[:, n * HALF:(n + 1) * HALF], w2_sb[:, k, n * P:(n + 1) * P],
                                                h1_sb[:, k, :], start=(k == 0), stop=(k == KH1 - 1))
                last.then_inc(h2_done, 1)

            def layer3(h):
                pe.wait_ge(h2_ready, h + 1)
                for k in range(KH2):
                    last = nc.tensor.matmul(h2_ps[0:1, KH2 * HALF:(KH2 + 1) * HALF], w3_sb[:, k:k + 1], h2_sb[:, k, :],
                                            start=(k == 0), stop=(k == KH2 - 1))
                last.then_inc(y_done, 1)

            def half(h, parity, first, last):
                for i in range(PAIRS):
                    transposes(h, i)
                    if i:
                        gram(h, i - 1, first)
                    elif not first:
                        gram(h - 1, PAIRS - 1, False)
                    if not first:
                        if i == 2:
                            layer1(h - 1, 1 - parity)
                        if i == 4:
                            layer2(h - 1)
                        if i == 6:
                            layer3(h - 1)

            for free_at_first in (h1_done, h2_done, y_done):
                nc.tensor.nop().then_inc(free_at_first, 1)
            pe.wait_ge(identity_loaded, 16)
            halves(nc.tensor, half)
            gram(NH - 1, PAIRS - 1, False)
            layer1(NH - 1, 1)
            layer2(NH - 1)
            layer3(NH - 1)


def kernel(**inputs):
    import concourse.bacc as bacc
    from concourse.bass_utils import run_bass_kernel_spmd

    tables = [np.asarray(inputs[f"tbl_{f}"]) for f in range(F)]
    first_row = np.concatenate([[0], np.cumsum([t.shape[0] for t in tables])[:-1]]).astype(np.int32)

    w1 = np.asarray(inputs["W_top1"])
    n, m = np.triu_indices(F, k=1)
    w1z = np.zeros((P, MM, H1), w1.dtype)
    w1z[F * (m % Q) + n, m // Q] = w1[:len(n)]

    arrays = {
        "table": np.concatenate(tables),
        "ids": np.ascontiguousarray(np.asarray(inputs["ids"]).reshape(B // J, P).T),
        "base": np.repeat(np.tile(first_row, J)[:, None], B // J, axis=1),
        "eye": np.eye(P, dtype=np.float32),
        "ctx_t": np.ascontiguousarray(np.asarray(inputs["dense_ctx"]).T),
        "w1z": w1z,
        "w1c": np.ascontiguousarray(w1[len(n):]),
        "b1": np.ascontiguousarray(np.asarray(inputs["b_top1"]).reshape(KH1, P).T),
        "w2": np.asarray(inputs["W_top2"]),
        "b2": np.ascontiguousarray(np.asarray(inputs["b_top2"]).reshape(KH2, P).T),
        "w3": np.ascontiguousarray(np.asarray(inputs["W_top3"]).reshape(KH2, P).T),
    }
    nc = bacc.Bacc("TRN2", target_bir_lowering=False, num_devices=1)
    drams = [nc.dram_tensor(f"in_{name}", a.shape, mybir.dt.from_np(a.dtype), kind="ExternalInput").ap()
             for name, a in arrays.items()]
    y = nc.dram_tensor("out_y", (B, 1), F32, kind="ExternalOutput").ap()
    dlrm_tower(nc, *drams, y)
    result = run_bass_kernel_spmd(nc, [{f"in_{name}": a for name, a in arrays.items()}], core_ids=[0])
    return result.results[0]["out_y"]
```

```python
from contextlib import ExitStack

import concourse.bass as bass
import numpy as np
from concourse import mybir

F32 = mybir.dt.float32
I32 = mybir.dt.int32
ALU = mybir.AluOpType
ACT = mybir.ActivationFunctionType

P = 128
B = 512
F = 32
D = 256
KD = D // P
CTX = 16
H1, H2 = 512, 256
KH1, KH2 = H1 // P, H2 // P
J = P // F
N = 128
NQ = B // N
G = N // J
PAIRS = G // 2
UNIT = 4
UNITS = PAIRS // UNIT
SLOTS = 16
XT_SLOTS = 4
S = F // 2
Q = 4
MM = S // Q

LANE = np.arange(F)[:, None]
SLOT = np.arange(S)[None, :]
TAKES_UPPER = np.where(LANE < S, LANE >= SLOT, LANE - S < SLOT)


def quarters(engine, quarter):
    quarter(0, True)
    with engine.Fori(0, NQ - 2) as turn:
        quarter(turn + 1, False)
    quarter(NQ - 1, False)


def dlrm_tower(nc, table, ids, base, eye, takes_upper, ctx_t, w1z, w1c, b1, w2, b2, w3, y):
    with ExitStack() as stack:
        def sbuf(name, shape, dt=F32):
            return stack.enter_context(nc.sbuf_tensor(name, shape, dt))

        def psum(name, shape):
            return stack.enter_context(nc.psum_tensor(name, shape, F32))

        def sem(name):
            return stack.enter_context(nc.semaphore(name))

        ids_sb = sbuf("ids_sb", [P, B // J], I32)
        base_sb = sbuf("base_sb", [P, B // J], I32)
        row_number = sbuf("row_number", [P, B // J], I32)
        rows = sbuf("rows", [P, SLOTS, D])
        identity = sbuf("identity", [P, P])
        upper_sb = sbuf("upper_sb", [P, S, 2 * UNIT], I32)
        xt = sbuf("xt", [P, XT_SLOTS, 2, KD, P])
        z = sbuf("z", [P, MM, N])
        ctx_sb = sbuf("ctx_sb", [CTX, B])
        w1z_sb = sbuf("w1z_sb", [P, MM, H1])
        w1c_sb = sbuf("w1c_sb", [CTX, H1])
        w2_sb = sbuf("w2_sb", [P, KH1, H2])
        w3_sb = sbuf("w3_sb", [P, KH2])
        b1_sb = sbuf("b1_sb", [P, KH1])
        b2_sb = sbuf("b2_sb", [P, KH2])
        h1_sb = sbuf("h1_sb", [P, KH1, N])
        h2_sb = sbuf("h2_sb", [P, KH2, N])
        y_sb = sbuf("y_sb", [1, B])

        xt_ps = [psum(f"xt_ps{i}", [P, 2, KD, P]) for i in range(2)]
        gram_ps = [psum(f"gram_ps{i}", [P, 2 * UNIT, P]) for i in range(2)]
        mlp_ps = [psum(f"mlp_ps{i}", [P, 4, N]) for i in range(2)]
        h1_ps = [mlp_ps[k % 2][:, k // 2, :] for k in range(KH1)]
        h2_ps = [mlp_ps[k % 2][:, 2, :] for k in range(KH2)]
        y_ps = mlp_ps[0][0:1, 3, :]

        ids_loaded = sem("ids_loaded")
        base_loaded = sem("base_loaded")
        identity_loaded = sem("identity_loaded")
        upper_loaded = sem("upper_loaded")
        ctx_loaded = sem("ctx_loaded")
        w1_loaded = sem("w1_loaded")
        b1_loaded = sem("b1_loaded")
        w2_loaded = sem("w2_loaded")
        b2_loaded = sem("b2_loaded")
        w3_loaded = sem("w3_loaded")
        numbered = sem("numbered")
        rows_landed = [sem(f"rows_landed{i}") for i in range(SLOTS)]
        rows_transposed = sem("rows_transposed")
        xt_ready = [sem("xt_even_ready"), sem("xt_odd_ready")]
        gram_ready = sem("gram_ready")
        z_lower_ready = sem("z_lower_ready")
        z_lower_seen = sem("z_lower_seen")
        z_ready = sem("z_ready")
        h1_done = sem("h1_done")
        h1_ready = sem("h1_ready")
        h2_done = sem("h2_done")
        h2_ready = sem("h2_ready")
        y_done = sem("y_done")
        y_ready = sem("y_ready")
        y_stored = sem("y_stored")

        block = stack.enter_context(nc.Block())

        @block.sync
        def _(sp):
            sp.dma_start(ids_sb[:], ids).then_inc(ids_loaded, 16)
            sp.dma_start(identity[:], eye).then_inc(identity_loaded, 16)
            sp.dma_start(upper_sb[:], takes_upper).then_inc(upper_loaded, 16)
            sp.dma_start(ctx_sb[:], ctx_t).then_inc(ctx_loaded, 16)
            sp.dma_start(w1c_sb[:], w1c).then_inc(ctx_loaded, 16)
            sp.dma_start(w1z_sb[:], w1z).then_inc(w1_loaded, 16)
            sp.dma_start(b1_sb[:], b1).then_inc(b1_loaded, 16)
            sp.dma_start(w2_sb[:], w2.rearrange("(k p) n -> p k n", p=P)).then_inc(w2_loaded, 16)
            sp.dma_start(b2_sb[:], b2).then_inc(b2_loaded, 16)
            sp.dma_start(w3_sb[:], w3).then_inc(w3_loaded, 16)
            sp.wait_ge(y_ready, NQ)
            sp.dma_start(y.rearrange("b o -> o b"), y_sb[:]).then_inc(y_stored, 16)
            sp.wait_ge(y_stored, 16)

        @block.gpsimd
        def _(pool):
            pool.wait_ge(numbered, 1)
            for n in range(B // J):
                if n >= SLOTS:
                    pool.wait_ge(rows_transposed, n + 1 - SLOTS)
                nc.gpsimd.indirect_dma_start(
                    rows[:, n % SLOTS, :], None, table,
                    bass.IndirectOffsetOnAxis(ap=row_number[:, n:n + 1], axis=0),
                ).then_inc(rows_landed[n % SLOTS], 16)

        def copy_xt(engine, copy, t, i, first):
            if not first or i >= XT_SLOTS:
                engine.wait_ge(gram_ready, t * PAIRS + (i + 1 - XT_SLOTS))
            engine.wait_ge(rows_transposed, t * G + 2 * (i + 1))
            copy(xt[:, i % XT_SLOTS], xt_ps[i % 2][:]).then_inc(xt_ready[i % 2], 1)

        def regroup_steps(u, j):
            to = z[:].rearrange("p m (g j) -> p m g j", j=J)
            dots = gram_ps[u % 2][F * j:F * j + F, :, F * j:F * j + F].rearrange("p g (c m q) -> p c m g q", c=2, q=Q)
            upper = upper_sb[F * j:F * j + F].rearrange("p (m q) g -> p m q g", q=Q)
            for q in range(Q):
                yield (to[F * q:F * q + F, :, 2 * UNIT * u:2 * UNIT * (u + 1), j], dots[:, 0, :, :, q],
                       dots[:, 1, :, :, q], upper[:, :, q, :])

        @block.vector
        def _(dve):
            def regroup_upper(t, u):
                dve.wait_ge(upper_loaded, 16)
                for j in range(J):
                    dve.wait_ge(z_lower_ready, t * (UNITS * J) + (u * J + j + 1)).then_inc(z_lower_seen, 1)
                    for z_to, _, upper_dots, upper in regroup_steps(u, j):
                        last = nc.vector.copy_predicated(z_to, upper, upper_dots)
                last.then_inc(z_ready, 1)

            def relu2(t):
                dve.wait_ge(b2_loaded, 16)
                for k in range(KH2):
                    dve.wait_ge(h2_done, t * KH2 + (k + 1))
                    nc.vector.tensor_scalar(h2_sb[:, k, :], h2_ps[k], b2_sb[:, k:k + 1], 0.0, ALU.add,
                                            ALU.max).then_inc(h2_ready, 1)

            def keep_y(t):
                dve.wait_ge(y_done, t + 1)
                nc.vector.tensor_copy(y_sb[0:1, bass.ds(t * N, N)], y_ps).then_inc(y_ready, 1)

            def quarter(t, first):
                for i in range(0, PAIRS, 2):
                    copy_xt(dve, nc.vector.tensor_copy, t, i, first)
                    if i == 0 and not first:
                        regroup_upper(t - 1, UNITS - 1)
                    if i and i % UNIT == 0:
                        regroup_upper(t, i // UNIT - 1)
                    if i == 4 and not first:
                        relu2(t - 1)
                    if i == 6 and not first:
                        keep_y(t - 1)

            dve.wait_ge(ids_loaded, 16)
            dve.wait_ge(base_loaded, 16)
            nc.vector.tensor_tensor(row_number[:], ids_sb[:], base_sb[:], ALU.add).then_inc(numbered, 1)
            quarters(nc.vector, quarter)
            regroup_upper(NQ - 1, UNITS - 1)
            relu2(NQ - 1)
            keep_y(NQ - 1)

        @block.scalar
        def _(act):
            def regroup_lower(t, u):
                act.wait_ge(gram_ready, t * PAIRS + UNIT * (u + 1))
                for j in range(J):
                    for z_to, lower_dots, _, _ in regroup_steps(u, j):
                        last = nc.scalar.copy(z_to, lower_dots)
                    last.then_inc(z_lower_ready, 1)

            def relu1(t):
                act.wait_ge(b1_loaded, 16)
                for k in range(KH1):
                    act.wait_ge(h1_done, t * KH1 + (k + 1))
                    nc.scalar.activation(h1_sb[:, k, :], h1_ps[k], ACT.Relu,
                                         bias=b1_sb[:, k:k + 1]).then_inc(h1_ready, 1)

            def quarter(t, first):
                if not first:
                    regroup_lower(t - 1, UNITS - 1)
                for i in range(1, PAIRS, 2):
                    copy_xt(act, nc.scalar.copy, t, i, first)
                    if i == 1 and not first:
                        relu1(t - 1)
                    if i % UNIT == 3 and i < PAIRS - 1:
                        regroup_lower(t, i // UNIT)

            act.dma_start(base_sb[:], base).then_inc(base_loaded, 16)
            quarters(nc.scalar, quarter)
            regroup_lower(NQ - 1, UNITS - 1)
            relu1(NQ - 1)

        @block.tensor
        def _(pe):
            def transposes(t, i, first):
                if not first or i >= 2:
                    pe.wait_ge(xt_ready[i % 2], t * (PAIRS // 2) + i // 2)
                for r in range(2):
                    g = 2 * i + r
                    pe.wait_ge(rows_landed[g % SLOTS], t * (G // SLOTS * 16) + (g // SLOTS + 1) * 16)
                    for k in range(KD):
                        last = nc.tensor.transpose(xt_ps[i % 2][:, r, k, :], rows[:, g % SLOTS, k * P:(k + 1) * P],
                                                   identity[:])
                    last.then_inc(rows_transposed, 1)

            def gram(t, i, first):
                u = i // UNIT
                pe.wait_ge(xt_ready[i % 2], t * (PAIRS // 2) + (i // 2 + 1))
                if i % UNIT == 0 and (u >= 2 or not first):
                    pe.wait_ge(z_ready, t * UNITS + (u - 1))
                for r in range(2):
                    for k in range(KD):
                        x = xt[:, i % XT_SLOTS, r, k, :]
                        last = nc.tensor.matmul(gram_ps[u % 2][:, 2 * (i % UNIT) + r, :], x, x, start=(k == 0),
                                                stop=(k == KD - 1))
                last.then_inc(gram_ready, 1)

            def layer1(t):
                pe.wait_ge(ctx_loaded, 32)
                pe.wait_ge(w1_loaded, 16)
                pe.wait_ge(z_ready, (t + 1) * UNITS)
                for n in range(KH1):
                    if n >= 2:
                        pe.wait_ge(h1_ready, t * KH1 + (n - 1))
                    for m in range(MM):
                        nc.tensor.matmul(h1_ps[n], w1z_sb[:, m, n * P:(n + 1) * P], z[:, m, :], start=(m == 0),
                                         stop=False)
                    nc.tensor.matmul(h1_ps[n], w1c_sb[:, n * P:(n + 1) * P], ctx_sb[:, bass.ds(t * N, N)],
                                     start=False, stop=True).then_inc(h1_done, 1)

            def layer2(t):
                pe.wait_ge(w2_loaded, 16)
                pe.wait_ge(h1_ready, t * KH1 + (KH1 - 1))
                for n in range(KH2):
                    for k in range(KH1):
                        if n == 0 and k == KH1 - 1:
                            pe.wait_ge(h1_ready, t * KH1 + KH1)
                        last = nc.tensor.matmul(h2_ps[n], w2_sb[:, k, n * P:(n + 1) * P], h1_sb[:, k, :],
                                                start=(k == 0), stop=(k == KH1 - 1))
                    last.then_inc(h2_done, 1)

            def layer3(t):
                pe.wait_ge(w3_loaded, 16)
                for k in range(KH2):
                    pe.wait_ge(h2_ready, t * KH2 + (k + 1))
                    last = nc.tensor.matmul(y_ps, w3_sb[:, k:k + 1], h2_sb[:, k, :], start=(k == 0),
                                            stop=(k == KH2 - 1))
                last.then_inc(y_done, 1)

            def quarter(t, first):
                for i in range(PAIRS):
                    transposes(t, i, first)
                    if i:
                        gram(t, i - 1, first)
                    elif not first:
                        gram(t - 1, PAIRS - 1, False)
                    if not first:
                        if i == 2:
                            layer1(t - 1)
                        if i == 3:
                            layer2(t - 1)
                        if i == 5:
                            layer3(t - 1)

            pe.wait_ge(identity_loaded, 16)
            quarters(nc.tensor, quarter)
            gram(NQ - 1, PAIRS - 1, False)
            layer1(NQ - 1)
            layer2(NQ - 1)
            layer3(NQ - 1)


def kernel(**inputs):
    import concourse.bacc as bacc
    from concourse.bass_utils import run_bass_kernel_spmd

    tables = [np.asarray(inputs[f"tbl_{f}"]) for f in range(F)]
    first_row = np.concatenate([[0], np.cumsum([t.shape[0] for t in tables])[:-1]]).astype(np.int32)

    w1 = np.asarray(inputs["W_top1"])
    pair_row = np.zeros((F, F), np.int64)
    pair_row[np.triu_indices(F, k=1)] = np.arange(F * (F - 1) // 2)
    w1z = np.zeros((P, MM, H1), w1.dtype)
    for lane in range(F):
        for slot in range(S):
            other = slot + S * int(TAKES_UPPER[lane, slot])
            if lane != other and not (lane >= S and other == lane - S):
                w1z[F * (slot % Q) + lane, slot // Q] = w1[pair_row[min(lane, other), max(lane, other)]]

    arrays = {
        "table": np.concatenate(tables),
        "ids": np.ascontiguousarray(np.asarray(inputs["ids"]).reshape(B // J, P).T),
        "base": np.repeat(np.tile(first_row, J)[:, None], B // J, axis=1),
        "eye": np.eye(P, dtype=np.float32),
        "takes_upper": np.repeat(np.tile(TAKES_UPPER.astype(np.int32), (J, 1))[:, :, None], 2 * UNIT, axis=2),
        "ctx_t": np.ascontiguousarray(np.asarray(inputs["dense_ctx"]).T),
        "w1z": w1z,
        "w1c": np.ascontiguousarray(w1[F * (F - 1) // 2:]),
        "b1": np.ascontiguousarray(np.asarray(inputs["b_top1"]).reshape(KH1, P).T),
        "w2": np.asarray(inputs["W_top2"]),
        "b2": np.ascontiguousarray(np.asarray(inputs["b_top2"]).reshape(KH2, P).T),
        "w3": np.ascontiguousarray(np.asarray(inputs["W_top3"]).reshape(KH2, P).T),
    }
    nc = bacc.Bacc("TRN2", target_bir_lowering=False, num_devices=1)
    drams = [nc.dram_tensor(f"in_{name}", a.shape, mybir.dt.from_np(a.dtype), kind="ExternalInput").ap()
             for name, a in arrays.items()]
    y = nc.dram_tensor("out_y", (B, 1), F32, kind="ExternalOutput").ap()
    dlrm_tower(nc, *drams, y)
    result = run_bass_kernel_spmd(nc, [{f"in_{name}": a for name, a in arrays.items()}], core_ids=[0])
    return result.results[0]["out_y"]
```

```python
from contextlib import ExitStack

import concourse.bass as bass
import numpy as np
from concourse import mybir

F32 = mybir.dt.float32
I32 = mybir.dt.int32
ALU = mybir.AluOpType
ACT = mybir.ActivationFunctionType

P = 128
B = 512
F = 32
D = 256
KD = D // P
CTX = 16
H1, H2 = 512, 256
KH1, KH2 = H1 // P, H2 // P
J = P // F
N = 128
NQ = B // N
G = N // J
UNIT = 8
UNITS = G // UNIT
SLOTS = 16
XT_SLOTS = 8
S = F // 2
Q = 4
MM = S // Q

CELLS = [(j, q) for j in range(J) for q in range(Q)]
DVE_CELLS, ACT_CELLS = CELLS[:10], CELLS[10:]

LANE = np.arange(F)[:, None]
SLOT = np.arange(S)[None, :]
TAKES_UPPER = np.where(LANE < S, LANE >= SLOT, LANE - S < SLOT)


LAYER1 = 4
LAYER2 = {False: [5, 5], True: [25, 27]}
LAYER3 = {False: 7, True: 29}


def quarters(engine, quarter):
    quarter(0, True, False)
    with engine.Fori(0, NQ - 2) as turn:
        quarter(turn + 1, False, False)
    quarter(NQ - 1, False, True)


def dlrm_tower(nc, table, ids, eye, takes_upper, ctx_t, w1z, w1c, b1, w2, b2, w3, y):
    with ExitStack() as stack:
        def sbuf(name, shape, dt=F32):
            return stack.enter_context(nc.sbuf_tensor(name, shape, dt))

        def psum(name, shape):
            return stack.enter_context(nc.psum_tensor(name, shape, F32))

        def sem(name):
            return stack.enter_context(nc.semaphore(name))

        ids_sb = sbuf("ids_sb", [P, B // J + 1], I32)
        row_number = sbuf("row_number", [P, B // J], I32)
        rows = sbuf("rows", [P, SLOTS, D])
        identity = sbuf("identity", [P, P])
        upper_sb = sbuf("upper_sb", [P, UNIT, S], I32)
        xt = sbuf("xt", [P, XT_SLOTS, KD, P])
        slots = sbuf("slots", [P, 2, UNIT, S])
        z = sbuf("z", [P, MM, N])
        ctx_sb = sbuf("ctx_sb", [CTX, B])
        w1z_sb = sbuf("w1z_sb", [P, MM, H1])
        w1c_sb = sbuf("w1c_sb", [CTX, H1])
        w2_sb = sbuf("w2_sb", [P, KH1, H2])
        w3_sb = sbuf("w3_sb", [P, KH2])
        b1_sb = sbuf("b1_sb", [P, KH1])
        b2_sb = sbuf("b2_sb", [P, KH2])
        h1_sb = sbuf("h1_sb", [P, KH1, N])
        h2_sb = sbuf("h2_sb", [P, KH2, N])
        y_sb = sbuf("y_sb", [1, B])

        xt_ps = [psum(f"xt_ps{i}", [P, 2 * KD, P])[:, 0:KD, :] for i in range(2)]
        gram_ps = [psum(f"gram_ps{i}", [P, 2 * UNIT, F])[:, 0:UNIT, :] for i in range(2)]
        mlp_ps = [psum(f"mlp_ps{i}", [P, 4, N]) for i in range(2)]
        h1_ps = [mlp_ps[k % 2][:, k // 2, :] for k in range(KH1)]
        h2_ps = [mlp_ps[k % 2][:, 2, :] for k in range(KH2)]
        y_ps = mlp_ps[0][0:1, 3, :]

        ids_loaded = sem("ids_loaded")
        identity_loaded = sem("identity_loaded")
        upper_loaded = sem("upper_loaded")
        ctx_loaded = sem("ctx_loaded")
        w1_loaded = sem("w1_loaded")
        b1_loaded = sem("b1_loaded")
        w2_loaded = sem("w2_loaded")
        b2_loaded = sem("b2_loaded")
        w3_loaded = sem("w3_loaded")
        numbered = sem("numbered")
        rows_landed = [sem(f"rows_landed{i}") for i in range(SLOTS)]
        rows_transposed = sem("rows_transposed")
        xt_ready = [sem("xt_even_ready"), sem("xt_odd_ready")]
        gram_ready = sem("gram_ready")
        lower_ready = sem("lower_ready")
        lower_seen = sem("lower_seen")
        slots_ready = sem("slots_ready")
        z_dve = sem("z_dve")
        z_act = sem("z_act")
        h1_done = sem("h1_done")
        h1_ready = sem("h1_ready")
        h2_done = sem("h2_done")
        h2_ready = sem("h2_ready")
        y_done = sem("y_done")
        y_ready = sem("y_ready")
        y_stored = sem("y_stored")

        block = stack.enter_context(nc.Block())

        @block.sync
        def _(sp):
            sp.dma_start(ids_sb[:], ids).then_inc(ids_loaded, 16)
            sp.dma_start(identity[:], eye).then_inc(identity_loaded, 16)
            sp.dma_start(upper_sb[:], takes_upper).then_inc(upper_loaded, 16)
            sp.dma_start(ctx_sb[:], ctx_t).then_inc(ctx_loaded, 16)
            sp.dma_start(w1c_sb[:], w1c).then_inc(ctx_loaded, 16)
            sp.dma_start(w1z_sb[:], w1z).then_inc(w1_loaded, 16)
            sp.dma_start(b1_sb[:], b1).then_inc(b1_loaded, 16)
            sp.dma_start(w2_sb[:], w2.rearrange("(k p) n -> p k n", p=P)).then_inc(w2_loaded, 16)
            sp.dma_start(b2_sb[:], b2).then_inc(b2_loaded, 16)
            sp.dma_start(w3_sb[:], w3).then_inc(w3_loaded, 16)
            sp.wait_ge(y_ready, NQ)
            sp.dma_start(y.rearrange("b o -> o b"), y_sb[:]).then_inc(y_stored, 16)
            sp.wait_ge(y_stored, 16)

        @block.gpsimd
        def _(pool):
            pool.wait_ge(numbered, 1)
            for n in range(B // J):
                if n >= SLOTS:
                    pool.wait_ge(rows_transposed, n + 1 - SLOTS)
                nc.gpsimd.indirect_dma_start(
                    rows[:, n % SLOTS, :], None, table,
                    bass.IndirectOffsetOnAxis(ap=row_number[:, n:n + 1], axis=0),
                ).then_inc(rows_landed[n % SLOTS], 16)

        def copy_xt(engine, copy, t, g, first):
            if not first or g >= XT_SLOTS:
                engine.wait_ge(gram_ready, t * G + (g + 1 - XT_SLOTS))
            engine.wait_ge(rows_transposed, t * G + (g + 1))
            copy(xt[:, g % XT_SLOTS], xt_ps[g % 2]).then_inc(xt_ready[g % 2], 1)

        def spread(engine, copy, cells, done, t, u):
            engine.wait_ge(slots_ready, t * UNITS + (u + 1))
            to = z[:].rearrange("p m (g j) -> p m g j", j=J)
            for j, q in cells:
                held = slots[F * j:F * j + F, u % 2].rearrange("p g (m q) -> p m g q", q=Q)
                last = copy(to[F * q:F * q + F, :, UNIT * u:UNIT * (u + 1), j], held[:, :, :, q])
            last.then_inc(done, 1)

        @block.vector
        def _(dve):
            def take_upper(t, u):
                dve.wait_ge(upper_loaded, 16)
                dve.wait_ge(lower_ready, t * UNITS + (u + 1)).then_inc(lower_seen, 1)
                nc.vector.copy_predicated(slots[:, u % 2], upper_sb[:], gram_ps[u % 2][:, :, S:F]).then_inc(slots_ready, 1)

            def relu2(t, chunks=range(KH2)):
                dve.wait_ge(b2_loaded, 16)
                for k in chunks:
                    dve.wait_ge(h2_done, t * KH2 + (k + 1))
                    nc.vector.tensor_scalar(h2_sb[:, k, :], h2_ps[k], b2_sb[:, k:k + 1], 0.0, ALU.add,
                                            ALU.max).then_inc(h2_ready, 1)

            def keep_y(t):
                dve.wait_ge(y_done, t + 1)
                nc.vector.tensor_copy(y_sb[0:1, bass.ds(t * N, N)], y_ps).then_inc(y_ready, 1)

            def quarter(t, first, last):
                for g in range(0, G, 2):
                    copy_xt(dve, nc.vector.tensor_copy, t, g, first)
                    if g == 0 and not first:
                        take_upper(t - 1, UNITS - 1)
                        spread(dve, nc.vector.tensor_copy, DVE_CELLS, z_dve, t - 1, UNITS - 1)
                    if not first:
                        for k in range(KH2):
                            if g == 1 + LAYER2[last][k]:
                                relu2(t - 1, [k])
                        if g == 1 + LAYER3[last]:
                            keep_y(t - 1)
                    if g and g % UNIT == 0:
                        take_upper(t, g // UNIT - 1)
                        spread(dve, nc.vector.tensor_copy, DVE_CELLS, z_dve, t, g // UNIT - 1)

            dve.wait_ge(ids_loaded, 16)
            nc.vector.tensor_tensor(row_number[:], ids_sb[:, 0:B // J],
                                    ids_sb[:, B // J:B // J + 1].broadcast_to([P, B // J]), ALU.add).then_inc(numbered, 1)
            quarters(nc.vector, quarter)
            take_upper(NQ - 1, UNITS - 1)
            spread(dve, nc.vector.tensor_copy, DVE_CELLS, z_dve, NQ - 1, UNITS - 1)
            relu2(NQ - 1)
            keep_y(NQ - 1)

        @block.scalar
        def _(act):
            def take_lower(t, u):
                act.wait_ge(gram_ready, t * G + UNIT * (u + 1))
                nc.scalar.copy(slots[:, u % 2], gram_ps[u % 2][:, :, 0:S]).then_inc(lower_ready, 1)

            def relu1(t):
                act.wait_ge(b1_loaded, 16)
                for k in range(KH1):
                    act.wait_ge(h1_done, t * KH1 + (k + 1))
                    nc.scalar.activation(h1_sb[:, k, :], h1_ps[k], ACT.Relu,
                                         bias=b1_sb[:, k:k + 1]).then_inc(h1_ready, 1)

            def quarter(t, first, last):
                if not first:
                    take_lower(t - 1, UNITS - 1)
                for g in range(1, G, 2):
                    copy_xt(act, nc.scalar.copy, t, g, first)
                    if g == 1 and not first:
                        spread(act, nc.scalar.copy, ACT_CELLS, z_act, t - 1, UNITS - 1)
                    if g == 3 and not first:
                        relu1(t - 1)
                    if g % UNIT == UNIT - 1 and g < G - 1:
                        take_lower(t, g // UNIT)
                    if g > UNIT and g % UNIT == 1:
                        spread(act, nc.scalar.copy, ACT_CELLS, z_act, t, g // UNIT - 1)

            quarters(nc.scalar, quarter)
            take_lower(NQ - 1, UNITS - 1)
            spread(act, nc.scalar.copy, ACT_CELLS, z_act, NQ - 1, UNITS - 1)
            relu1(NQ - 1)

        @block.tensor
        def _(pe):
            def transposes(t, g, first):
                if not first or g >= 2:
                    pe.wait_ge(xt_ready[g % 2], t * (G // 2) + g // 2)
                pe.wait_ge(rows_landed[g % SLOTS], t * (G // SLOTS * 16) + (g // SLOTS + 1) * 16)
                for k in range(KD):
                    last = nc.tensor.transpose(xt_ps[g % 2][:, k, :], rows[:, g % SLOTS, k * P:(k + 1) * P],
                                               identity[:])
                last.then_inc(rows_transposed, 1)

            def gram(t, g, first):
                u = g // UNIT
                pe.wait_ge(xt_ready[g % 2], t * (G // 2) + (g // 2 + 1))
                if g % UNIT == 0 and (u >= 2 or not first):
                    pe.wait_ge(slots_ready, t * UNITS + (u - 1))
                for j in range(J):
                    for k in range(KD):
                        x = xt[:, g % XT_SLOTS, k, F * j:F * j + F]
                        last = nc.tensor.matmul(gram_ps[u % 2][F * j:F * j + F, g % UNIT, :], x, x, start=(k == 0),
                                                stop=(k == KD - 1))
                last.then_inc(gram_ready, 1)

            def layer1(t, last=False):
                if last:
                    pe.wait_ge(y_ready, t)
                pe.wait_ge(ctx_loaded, 32)
                for n in range(KH1):
                    nc.tensor.matmul(h1_ps[n], w1c_sb[:, n * P:(n + 1) * P], ctx_sb[:, bass.ds(t * N, N)],
                                     start=(n < 2), stop=False, skip_group_check=True)
                pe.wait_ge(w1_loaded, 16)
                pe.wait_ge(z_dve, (t + 1) * UNITS)
                pe.wait_ge(z_act, (t + 1) * UNITS)
                for n in range(KH1):
                    if n >= 2:
                        pe.wait_ge(h1_ready, t * KH1 + (n - 1))
                    for m in range(MM):
                        done = nc.tensor.matmul(h1_ps[n], w1z_sb[:, m, n * P:(n + 1) * P], z[:, m, :], start=False,
                                                stop=(m == MM - 1), skip_group_check=True)
                    done.then_inc(h1_done, 1)

            def layer2(t, chunks=range(KH2)):
                pe.wait_ge(w2_loaded, 16)
                pe.wait_ge(h1_ready, t * KH1 + (KH1 - 1))
                for n in chunks:
                    for k in range(KH1):
                        if n == 0 and k == KH1 - 1:
                            pe.wait_ge(h1_ready, t * KH1 + KH1)
                        last = nc.tensor.matmul(h2_ps[n], w2_sb[:, k, n * P:(n + 1) * P], h1_sb[:, k, :],
                                                start=(k == 0), stop=(k == KH1 - 1))
                    last.then_inc(h2_done, 1)

            def layer3(t):
                pe.wait_ge(w3_loaded, 16)
                for k in range(KH2):
                    pe.wait_ge(h2_ready, t * KH2 + (k + 1))
                    last = nc.tensor.matmul(y_ps, w3_sb[:, k:k + 1], h2_sb[:, k, :], start=(k == 0),
                                            stop=(k == KH2 - 1))
                last.then_inc(y_done, 1)

            def quarter(t, first, last):
                for g in range(G):
                    transposes(t, g, first)
                    if g:
                        gram(t, g - 1, first)
                    elif not first:
                        gram(t - 1, G - 1, False)
                    if not first:
                        if g == LAYER1:
                            layer1(t - 1)
                        for n in range(KH2):
                            if g == LAYER2[last][n]:
                                layer2(t - 1, [n])
                        if g == LAYER3[last]:
                            layer3(t - 1)

            pe.wait_ge(identity_loaded, 16)
            quarters(nc.tensor, quarter)
            gram(NQ - 1, G - 1, False)
            layer1(NQ - 1, last=True)
            layer2(NQ - 1)
            layer3(NQ - 1)


def kernel(**inputs):
    import concourse.bacc as bacc
    from concourse.bass_utils import run_bass_kernel_spmd

    tables = [np.asarray(inputs[f"tbl_{f}"]) for f in range(F)]
    first_row = np.concatenate([[0], np.cumsum([t.shape[0] for t in tables])[:-1]]).astype(np.int32)

    w1 = np.asarray(inputs["W_top1"])
    pair_row = np.zeros((F, F), np.int64)
    pair_row[np.triu_indices(F, k=1)] = np.arange(F * (F - 1) // 2)
    w1z = np.zeros((P, MM, H1), w1.dtype)
    for lane in range(F):
        for slot in range(S):
            other = slot + S * int(TAKES_UPPER[lane, slot])
            if lane != other and not (lane >= S and other == lane - S):
                w1z[F * (slot % Q) + lane, slot // Q] = w1[pair_row[min(lane, other), max(lane, other)]]

    arrays = {
        "table": np.concatenate(tables),
        "ids": np.concatenate([np.asarray(inputs["ids"]).reshape(B // J, P).T, np.tile(first_row, J)[:, None]], axis=1),
        "eye": np.eye(P, dtype=np.float32),
        "takes_upper": np.repeat(np.tile(TAKES_UPPER.astype(np.int32), (J, 1))[:, None, :], UNIT, axis=1),
        "ctx_t": np.ascontiguousarray(np.asarray(inputs["dense_ctx"]).T),
        "w1z": w1z,
        "w1c": np.ascontiguousarray(w1[F * (F - 1) // 2:]),
        "b1": np.ascontiguousarray(np.asarray(inputs["b_top1"]).reshape(KH1, P).T),
        "w2": np.asarray(inputs["W_top2"]),
        "b2": np.ascontiguousarray(np.asarray(inputs["b_top2"]).reshape(KH2, P).T),
        "w3": np.ascontiguousarray(np.asarray(inputs["W_top3"]).reshape(KH2, P).T),
    }
    nc = bacc.Bacc("TRN2", target_bir_lowering=False, num_devices=1)
    drams = [nc.dram_tensor(f"in_{name}", a.shape, mybir.dt.from_np(a.dtype), kind="ExternalInput").ap()
             for name, a in arrays.items()]
    y = nc.dram_tensor("out_y", (B, 1), F32, kind="ExternalOutput").ap()
    dlrm_tower(nc, *drams, y)
    result = run_bass_kernel_spmd(nc, [{f"in_{name}": a for name, a in arrays.items()}], core_ids=[0])
    return result.results[0]["out_y"]
```
